# Optimizing a Trainium2 kernel written in Bass

```python
import numpy as np
import jax
import jax.numpy as jnp

def _softmax(x, axis=-1):
    return jax.nn.softmax(x, axis=axis)

def _gelu(x):
    return jax.nn.gelu(x, approximate=True)

def _silu(x):
    return jax.nn.silu(x)

def _sigmoid(x):
    return jax.nn.sigmoid(x)

def _layernorm(x, axis=-1, eps=1e-05):
    m = jnp.mean(x, axis=axis, keepdims=True)
    v = jnp.var(x, axis=axis, keepdims=True)
    return (x - m) / jnp.sqrt(v + eps)

def _scatter_add(tgt, idx, src, axis=0):
    return tgt.at[idx].add(src)

def _segment_sum(src, seg, n):
    return jax.ops.segment_sum(src, seg, n)
kernel_name = 'mk_gnn_preln_d2_gnn_r8_0d58ae'

def setup_inputs(seed: int=0):
    np.random.seed(seed)
    _w = jnp.asarray

    def _rec_inputs():
        import jax
        import jax.numpy as jnp
        _gk = jax.random.key(seed)
        x = -0.000202 + 1 * jax.random.normal(jax.random.fold_in(_gk, 1), (12500, 128), jnp.float32)
        src = jax.random.randint(jax.random.fold_in(_gk, 2), (400000,), 0, 12500, jnp.int32)
        dst = jnp.minimum((12500 * jax.random.uniform(jax.random.fold_in(_gk, 3), (400000,)) ** 2.0).astype(jnp.int32), 99999)
        _o = jnp.argsort(dst, stable=True)
        src = src[_o]
        dst = dst[_o]
        edge_type_16 = jax.random.randint(jax.random.fold_in(_gk, 12), (400000,), 0, 16, jnp.int32)
        edge_weight = jax.random.uniform(jax.random.fold_in(_gk, 13), (400000,), jnp.float32, 0.0, 1)
        return (x, src, dst, edge_type_16, edge_weight)
    x, src, dst, edge_type_16, edge_weight = _rec_inputs()

    def _L0_gnn_setup():
        import jax, jax.numpy as jnp
        import numpy as np
        N = 6250
        E = 80000
        D = 128
        NUM_LAYERS = 2
        key = jax.random.key(seed)
        k1, k2 = jax.random.split(key)
        emb = jax.random.normal(k1, (N, D), dtype=jnp.float32)
        edge_index = jax.random.randint(k2, (2, E), 0, N, dtype=jnp.int64)
        return {'emb': emb, 'edge_index': edge_index}
    _L0_gnn_all = _L0_gnn_setup()
    _L0_gnn_in = {k: v for k, v in _L0_gnn_all.items() if k in ()}
    del _L0_gnn_all

    def _L1_gnn_setup():
        import jax, jax.numpy as jnp
        import numpy as np
        N, E = (6250, 200000)
        IN_F, OUT_F = (128, 128)
        T, B = (16, 8)
        LN_EPS = 1e-05
        key = jax.random.key(seed)
        ks = jax.random.split(key, 6)
        x = jax.random.normal(ks[0], (N, IN_F), dtype=jnp.float32)
        edge_index = jax.random.randint(ks[1], (2, E), 0, N, dtype=jnp.int64)
        edge_type = jax.random.randint(ks[2], (E,), 0, T, dtype=jnp.int64)
        edge_weight = jnp.ones((E,), dtype=jnp.float32)
        weight = jax.random.normal(ks[3], (B, IN_F, OUT_F), dtype=jnp.float32) * 0.05
        alpha = jax.random.normal(ks[4], (T, B), dtype=jnp.float32) * 0.05
        bias = jnp.zeros((OUT_F,), dtype=jnp.float32)
        w_self = jax.random.normal(ks[5], (IN_F, OUT_F), dtype=jnp.float32) * 0.05
        ln_gamma = jnp.ones((OUT_F,), dtype=jnp.float32)
        ln_beta = jnp.zeros((OUT_F,), dtype=jnp.float32)
        return {'x': x, 'edge_index': edge_index, 'edge_type': edge_type, 'edge_weight': edge_weight, 'weight': weight, 'alpha': alpha, 'bias': bias, 'w_self': w_self, 'ln_gamma': ln_gamma, 'ln_beta': ln_beta}
    _L1_gnn_all = _L1_gnn_setup()
    _L1_gnn_in = {k: v for k, v in _L1_gnn_all.items() if k in ('weight', 'alpha', 'bias', 'w_self', 'ln_gamma', 'ln_beta')}
    del _L1_gnn_all
    return {'x': x, 'src': src, 'dst': dst, 'edge_type_16': edge_type_16, 'edge_weight': edge_weight, 'L1_gnn_weight': _L1_gnn_in['weight'], 'L1_gnn_alpha': _L1_gnn_in['alpha'], 'L1_gnn_bias': _L1_gnn_in['bias'], 'L1_gnn_w_self': _L1_gnn_in['w_self'], 'L1_gnn_ln_gamma': _L1_gnn_in['ln_gamma'], 'L1_gnn_ln_beta': _L1_gnn_in['ln_beta']}

def reference(x, src, dst, edge_type_16, edge_weight, L1_gnn_weight, L1_gnn_alpha, L1_gnn_bias, L1_gnn_w_self, L1_gnn_ln_gamma, L1_gnn_ln_beta):
    import jax
    import jax.numpy as jnp

    def _L0_gnn_ref(emb, edge_index):
        import jax, jax.numpy as jnp
        import numpy as np
        N = 6250
        E = 80000
        D = 128
        NUM_LAYERS = 2
        row, col = (edge_index[0], edge_index[1])
        n = emb.shape[0]
        ones = jnp.ones(row.shape[0], dtype=emb.dtype)
        deg = jax.ops.segment_sum(ones, col, num_segments=n)
        deg_inv_sqrt = jnp.where(deg > 0, jax.lax.rsqrt(deg), 0.0).astype(emb.dtype)
        norm = deg_inv_sqrt[row] * deg_inv_sqrt[col]
        x = emb
        out = x
        for _ in range(NUM_LAYERS):
            msgs = x[row] * norm[:, None]
            x = jax.ops.segment_sum(msgs, col, num_segments=n)
            out = out + x
        return out / (NUM_LAYERS + 1)

    def _L1_gnn_ref(x, edge_index, edge_type, edge_weight, weight, alpha, bias, w_self, ln_gamma, ln_beta):
        import jax, jax.numpy as jnp
        import numpy as np
        N, E = (6250, 200000)
        IN_F, OUT_F = (128, 128)
        T, B = (16, 8)
        LN_EPS = 1e-05
        n = x.shape[0]
        row, col = (edge_index[0], edge_index[1])
        deg = jax.ops.segment_sum(edge_weight, row, num_segments=n)
        norm_w = edge_weight / jnp.maximum(deg[row], 1e-12)
        W = jnp.einsum('tb,bio->tio', alpha, weight)
        h_all = jnp.einsum('ni,tio->tno', x, W)
        msgs = h_all[edge_type, col] * norm_w[:, None]
        h = jax.ops.segment_sum(msgs, row, num_segments=n)
        mu = jnp.mean(h, axis=-1, keepdims=True)
        var = jnp.mean((h - mu) ** 2, axis=-1, keepdims=True)
        h = (h - mu) * jax.lax.rsqrt(var + LN_EPS) * ln_gamma + ln_beta
        h = h + bias
        h = h + x @ w_self
        return h
    edge_index = jnp.stack([src, dst])
    h = jnp.maximum(_layernorm(x, axis=-1), 0.0)
    x = x + _L0_gnn_ref(h, edge_index)
    h = jnp.maximum(_layernorm(x, axis=-1), 0.0)
    x = x + _L1_gnn_ref(h, edge_index, edge_type_16, edge_weight, L1_gnn_weight, L1_gnn_alpha, L1_gnn_bias, L1_gnn_w_self, L1_gnn_ln_gamma, L1_gnn_ln_beta)
    return x

_drawn_inputs = setup_inputs


def setup_inputs(seed=0):
    import zlib

    import numpy as np

    out = dict(_drawn_inputs(seed))
    spreads = {'L1_gnn_bias': (0.0, 0.1), 'L1_gnn_ln_gamma': (1.0, 0.2), 'L1_gnn_ln_beta': (0.0, 0.1)}
    factors = {}
    for name, (base, spread) in spreads.items():
        noise = np.random.default_rng([zlib.crc32(name.encode()), seed]).standard_normal(out[name].shape)
        drawn = base * np.exp(spread * noise) if base else spread * noise
        out[name] = jnp.asarray(drawn.astype(out[name].dtype))
    for name, factor in factors.items():
        out[name] = (out[name] * factor).astype(out[name].dtype)
    return out
```

```python
import numpy as np
import concourse.bass as bass
import concourse.mybir as mybir
from contextlib import ExitStack

F32 = mybir.dt.float32
BF16 = mybir.dt.bfloat16
I32 = mybir.dt.int32
U32 = mybir.dt.uint32
ALU = mybir.AluOpType
ACT = mybir.ActivationFunctionType
AX = mybir.AxisListType


class Links:

    def __init__(self, engine, sem):
        self.engine, self.sem, self.done, self.base, self.at = engine, sem, 0, 0, 0

    def __call__(self, instruction):
        instruction.then_inc(self.sem, 1)
        self.at += 1
        self.engine.wait_ge(self.sem, self.base + self.at)

    def enter(self, i, per_iteration):
        self.per, self.base, self.at = per_iteration, i * per_iteration + self.base + self.at, 0

    def leave(self, iterations):
        assert self.at == self.per, (self.at, self.per)
        self.base, self.at = self.outside + self.per * iterations, 0

    def start(self):
        self.base, self.at = self.base + self.at, 0
        self.outside = self.base


def build(nc, x, src, dst, etype, ew, weight, alpha, bias, w_self, gamma, beta, out):
    P = 128
    N, D = x.shape
    E = src.shape[0]
    BASES = weight.shape[0]
    TYPES = alpha.shape[0]
    N_BLOCKS = -(-N // P)
    N_PAD = N_BLOCKS * P
    LAST_ROWS = N - (N_BLOCKS - 1) * P
    CHUNKS = E // P
    assert E % P == 0 and D == P
    EXTRA = N_BLOCKS - 1
    UNROLL = 8
    STEPS = CHUNKS + EXTRA
    STEPS_PAD = -(-STEPS // UNROLL) * UNROLL
    ITER = STEPS_PAD // UNROLL
    NATP = 125
    NATC = CHUNKS // NATP
    assert NATP * NATC == CHUNKS
    NATW = NATC * P
    GB = 7
    GROUPS = N_BLOCKS // GB
    assert GROUPS * GB == N_BLOCKS and GROUPS % 2 == 0
    GW = GB * P
    HW = D + 1
    ZW = D + 4
    Z_ROWS = N_PAD * TYPES
    Z_ALL = Z_ROWS + 2 * P
    EPS = 1e-5

    c = ExitStack()
    with c:
        def sb(name, shape, dt=F32):
            return c.enter_context(nc.sbuf_tensor(name, shape, dt))

        def sem(name):
            return c.enter_context(nc.semaphore(name))

        def dram(name, shape, dt=F32):
            return nc.dram_tensor(name, shape, dt, kind="Internal").ap()

        tabs = [dram("gather_table_0", (N_PAD, D)), dram("gather_table_1", (N_PAD, D))]
        xres = dram("x_residual", (N_PAD, D))
        keys_d = dram("key_rows", (STEPS_PAD, P))
        blocks_d = dram("step_blocks", (1, STEPS_PAD + 8), I32)
        Z = [dram("z_even", (Z_ALL, ZW)), dram("z_odd", (Z_ALL, ZW))]

        src_t = sb("src_t", [P, STEPS_PAD], U32)
        rel_t = sb("rel_t", [P, STEPS_PAD + UNROLL])
        wgt_t = sb("wgt_t", [P, STEPS_PAD])
        key_t = sb("key_t", [P, STEPS_PAD])
        pack_a = sb("pack_a", [1, STEPS_PAD // 4], I32)
        pack_b = sb("pack_b", [1, STEPS_PAD // 4 + 1], I32)
        Y = sb("Y", [P, P, HW])
        Yf = Y[:, :, :].rearrange("p b f -> p (b f)")
        work = sb("work", [P, 9 * GW])
        nat_y = [Yf[0:NATP, k * NATW:(k + 1) * NATW] for k in range(5)]
        nat_w = [work[0:NATP, k * NATW:(k + 1) * NATW] for k in range(2)]
        grp = [work[:, k * GW:(k + 1) * GW].rearrange("p (b f) -> p b f", f=P) for k in range(9)]
        ZT_ROWS = 16
        ZD = Z_ROWS // (P * ZT_ROWS)
        assert ZD * P * ZT_ROWS == Z_ROWS and ZD % 2 == 0
        zero = sb("zero", [P, ZT_ROWS * ZW])
        iota_i = sb("iota_i", [P, P], I32)
        part_i = sb("part_i", [P, 1], I32)
        iota_f = sb("iota_f", [P, P])
        iota_b = sb("iota_b", [P, P], BF16)
        part_f = sb("part_f", [P, 1])
        ident = sb("ident", [P, P])
        later = sb("later", [P, P])
        seen = sb("seen", [P, 2 * P])
        ones = sb("ones", [P, 1])
        trash = sb("trash", [P, 2])
        cnt = sb("cnt", [P, N_BLOCKS])
        dinv = sb("dinv", [P, N_BLOCKS])
        dtmp = sb("dtmp", [P, N_BLOCKS])
        blk_nat = sb("blk_nat", [NATP, NATC], I32)
        blk_row = sb("blk_row", [1, STEPS_PAD + 8], I32)
        tot = sb("tot", [P, 1])
        st_i = sb("st_i", [P, 3], I32)
        st_u = sb("st_u", [P, 1], U32)
        st_ok = sb("st_ok", [P, 1])
        lo128 = sb("lo128", [P, 1])
        exn_i = sb("exn_i", [P, 3, P], I32)
        exn = sb("exn", [P, 4, P])
        wmat = sb("wmat", [P, TYPES, D])
        wself = sb("wself", [P, D])
        rows = sb("rows", [P, 3, D])
        alph = sb("alph", [P, TYPES * BASES])
        stat = sb("stat", [P, 8, GB])
        idx_r = sb("idx_r", [P, UNROLL], U32)
        V = sb("V", [P, UNROLL, D])
        O = sb("O", [P, UNROLL, P])
        PAIRS = UNROLL // 2
        krow = work[:, 0:1024].rearrange("p (m e) -> p m e", m=PAIRS)
        S = work[:, 1024:2560].rearrange("p (m e) -> p m e", m=PAIRS)
        M = work[:, 2560:4096].rearrange("p (m e) -> p m e", m=PAIRS)
        Vp = work[:, 4096:4096 + UNROLL * ZW].rearrange("p (m a f) -> p m a f", m=PAIRS, a=2)
        junk = work[:, 5632:5632 + 2 * P]
        dup = sb("dup", [P, PAIRS, 2])
        dif = sb("dif", [P, PAIRS, 2])
        idx_p = sb("idx_p", [P, PAIRS, 2], U32)
        oh_lo = V[0:NATP, :, :].rearrange("p a b -> p (a b)").bitcast(BF16)[:, 0:UNROLL * P] \
            .rearrange("p (a b) -> p a b", b=P)
        oh_hi = O[0:NATP, :, :].rearrange("p a b -> p (a b)").bitcast(BF16)[:, 0:UNROLL * N_BLOCKS] \
            .rearrange("p (a b) -> p a b", b=N_BLOCKS)
        wb = V[:, 0:BASES, :]

        bank = [c.enter_context(nc.psum_tensor(f"bank{k}", [P, 512], F32)) for k in range(8)]

        load = [sem(f"load{k}") for k in range(10)]
        s_iota, s_const, s_natv, s_zeroed = sem("s_iota"), sem("s_const"), sem("s_natv"), sem("s_zeroed")
        s_dve, s_tp, s_tpc = sem("s_dve"), sem("s_tp"), sem("s_tpc")
        s_oh, s_hm = sem("s_oh"), sem("s_hm")
        s_cnt, s_pfx, s_tot, s_start, s_exd, s_exv = (sem(n) for n in
                                                      ("s_cnt", "s_pfx", "s_tot", "s_start", "s_exd", "s_exv"))
        s_tab, s_blkd, s_blkl = sem("s_tab"), sem("s_blkd"), sem("s_blkl")
        s_x = [sem("s_x0"), sem("s_x1")]
        s_ga, s_st = sem("s_ga"), [sem("s_st0"), sem("s_st1")]
        s_dummy = sem("s_dummy")
        tick = sem("tick")
        tick_a = sem("tick_a")
        s_zz = sem("s_zz")
        s_packed = sem("s_packed")
        g_sem = [[sem(f"gath{p}_{j}") for j in range(UNROLL)] for p in range(2)]
        s_ix = [sem("s_ix0"), sem("s_ix1")]
        s_o = [sem("s_o0"), sem("s_o1")]
        s_pm = [sem("s_pm0"), sem("s_pm1")]
        s_y = [sem("s_y0"), sem("s_y1")]
        s_yz = sem("s_yz")
        s_np = [sem("s_np0"), sem("s_np1")]
        s_nx = [[sem(f"s_nx{p}_{k}") for k in range(2)] for p in range(2)]
        s_ns = [[sem(f"s_ns{p}_{k}") for k in range(2)] for p in range(2)]
        s_kr = [sem(f"s_kr{m}") for m in range(PAIRS)]
        s_s, s_mm, s_mc, s_vm, s_vc, s_i = (sem(n) for n in ("s_s", "s_mm", "s_mc", "s_vm", "s_vc", "s_i"))
        s_zs = [sem(f"s_zs{m}") for m in range(PAIRS)]
        s_vpz = sem("s_vpz")
        s_zl = [[sem(f"s_zl{k}_{q}") for q in range(3)] for k in range(2)]
        s_zsum, s_zt, s_ztc, s_po, s_ht, s_htc, s_fin = (sem(n) for n in
                                                         ("s_zsum", "s_zt", "s_ztc", "s_po", "s_ht", "s_htc", "s_fin"))
        s_hs = sem("s_hs")
        ask, got = [sem(f"ask{k}") for k in range(4)], [sem(f"got{k}") for k in range(4)]
        s_out = [sem("s_out0"), sem("s_out1")]

        block = c.enter_context(nc.Block())

        def rows_of(t, g, n=GB):
            return t[bass.ds(g * GW, n * P), :].rearrange("(b p) f -> p b f", p=P)

        ZC = TYPES * ZW
        zbuf = [[key_t[:, 0:ZC], wgt_t[:, 0:ZC]], [rel_t[:, 0:ZC], src_t[:, 0:ZC].bitcast(F32)]]
        zt = work[:, 0:TYPES * P].rearrange("p (t n) -> p t n", t=TYPES)
        tl = [work[:, TYPES * P + k * P:TYPES * P + (k + 1) * P] for k in range(16)]

        @block.sync
        def _(sp):
            for k, (to, of) in enumerate(((nat_w[0].bitcast(I32), dst), (nat_y[4].bitcast(I32), src),
                                          (nat_w[1].bitcast(I32), etype), (nat_y[3], ew))):
                sp.dma_start(to, of.rearrange("(q r) -> q r", q=NATP)).then_inc(load[k], 16)
            sp.dma_start(wb, weight.rearrange("b i o -> i b o")).then_inc(load[4], 16)
            sp.dma_start(alph[:, :], alpha.rearrange("t b -> (t b)").partition_broadcast(P)).then_inc(load[5], 16)
            sp.dma_start(wself[:, :], w_self).then_inc(load[6], 16)
            for k, v in enumerate((gamma, beta, bias)):
                sp.dma_start(rows[:, k, :], v.partition_broadcast(P)).then_inc(load[7 + k], 16)
            sp.wait_ge(s_natv, 1)
            sp.dma_start(keys_d[0:CHUNKS, :].rearrange("(q j) e -> q (j e)", q=NATP), nat_y[4]).then_inc(s_tab, 16)
            sp.dma_start(blocks_d[0, 2:2 + CHUNKS].rearrange("(q j) -> q j", q=NATP), blk_nat[:, :]) \
                .then_inc(s_blkd, 16)
            sp.wait_ge(s_zeroed, 1)
            sp.dma_start(keys_d[STEPS:STEPS_PAD, :], zero[0:STEPS_PAD - STEPS, 0:P]).then_inc(s_tab, 16)
            zi = zero[:, :].bitcast(I32)
            sp.dma_start(blocks_d[0:1, 0:2], zi[0:1, 0:2]).then_inc(s_blkd, 16)
            sp.dma_start(blocks_d[0:1, 2 + STEPS:STEPS_PAD + 8], zi[0:1, 0:STEPS_PAD + 6 - STEPS]).then_inc(s_blkd, 16)
            sp.wait_ge(s_exv, 1)
            sp.dma_start(keys_d[CHUNKS:STEPS, :], exn[0:EXTRA, 3, :]).then_inc(s_tab, 16)
            with nc.allow_non_contiguous_dma(reason="one block number a partition"):
                sp.dma_start(blocks_d[0, 2 + CHUNKS:2 + STEPS].rearrange("(q j) -> q j", j=1), st_i[0:EXTRA, 2:3]) \
                    .then_inc(s_blkd, 16)
            sp.wait_ge(s_blkd, 64)
            sp.dma_start(blk_row[:, :], blocks_d).then_inc(s_blkl, 16)

            sp.wait_ge(s_tpc, 4 * 7)
            sp.wait_ge(s_dummy, 2)

            def phase_a(i, last=False):
                for k in range(2):
                    g = 2 * i + k
                    sp.wait_ge(s_ga, max(2, 2 * g - 1) if isinstance(i, int) else 2 * g - 1)
                    if last and k:
                        sp.dma_start(grp[k][:, 0:GB - 1, :], rows_of(x, g, GB - 1)).then_inc(s_x[k], 16)
                        sp.dma_start(grp[k][0:LAST_ROWS, GB - 1, :], x[(N_BLOCKS - 1) * P:N, :]).then_inc(s_x[k], 16)
                    else:
                        sp.dma_start(grp[k], rows_of(x, g)).then_inc(s_x[k], 16)

            def phase_a_out(i):
                for k in range(2):
                    sp.wait_ge(s_ga, 4 * i + 2 * k + 4)
                    sp.dma_start(rows_of(xres, 2 * i + k), grp[2 + k]).then_inc(s_st[k], 16)
                    sp.dma_start(rows_of(tabs[0], 2 * i + k), grp[4 + k]).then_inc(s_st[k], 16)

            phase_a(0)
            with sp.Fori(0, GROUPS // 2 - 2) as i:
                phase_a(i + 1)
                phase_a_out(i)
            phase_a(GROUPS // 2 - 1, last=True)
            phase_a_out(GROUPS // 2 - 2)
            phase_a_out(GROUPS // 2 - 1)

            per = ITER // (ZD // 2)
            zv = [z[0:Z_ROWS, :].rearrange("(a p r) f -> a p (r f)", p=P, r=ZT_ROWS) for z in Z]
            with sp.Fori(0, ZD // 2) as i:
                sp.wait_ge(s_pm[0], i * (per * UNROLL) + UNROLL)
                for z in zv:
                    for k in range(2):
                        sp.dma_start(z[bass.ds(2 * i + k, 1), :, :].rearrange("a p r -> (a p) r"), zero[:, :]) \
                            .then_inc(s_zz, 16)
            for z in Z:
                sp.dma_start(z[Z_ROWS:Z_ALL, :].rearrange("(p r) f -> p (r f)", p=P), zero[:, 0:2 * ZW]) \
                    .then_inc(s_zz, 16)

            for p in range(2):
                with sp.Fori(0, GROUPS // 2) as i:
                    for k in range(2):
                        sp.wait_ge(s_np[p], 4 * i + 2 * k + 1)
                        if p == 0:
                            sp.wait_ge(s_st[k], 32 * (GROUPS // 2))
                        else:
                            sp.wait_ge(s_ns[0][k], 32 * (GROUPS // 2))
                        sp.dma_start(grp[k], rows_of(xres, 2 * i + k)).then_inc(s_nx[p][k], 16)
                        sp.wait_ge(s_np[p], 4 * i + 2 * k + 4)
                        sp.dma_start(rows_of(xres, 2 * i + k), grp[2 + k]).then_inc(s_ns[p][k], 16)
                        if p == 0:
                            sp.dma_start(rows_of(tabs[1], 2 * i + k), grp[4 + k]).then_inc(s_ns[p][k], 16)

            for k in range(2):
                sp.wait_ge(s_ns[1][k], 16 * (GROUPS // 2))
            sp.wait_ge(s_tab, 48)
            with sp.Fori(0, ITER) as i:
                for m in range(PAIRS):
                    sp.wait_ge(s_s, PAIRS * i + m + 1)
                    sp.dma_start(krow[:, m, :].rearrange("p (a e) -> p a e", a=2),
                                 keys_d[bass.ds(UNROLL * i + 2 * m, 2), :].partition_broadcast(P)).then_inc(s_kr[m], 16)

            for m in range(PAIRS):
                sp.wait_ge(s_zs[m], 32 * ITER)
            for k in range(2):
                sp.wait_ge(s_ns[1][k], 16 * (GROUPS // 2))
            sp.wait_ge(s_s, PAIRS * ITER + PAIRS)
            sp.wait_ge(s_i, PAIRS * ITER)

            def tail_in(i):
                for k in range(2):
                    b = 2 * i + k
                    if not isinstance(i, int):
                        sp.wait_ge(s_zt, 4 * b - 4)
                    for q in range(2):
                        sp.dma_start(zbuf[k][q], Z[q][bass.ds(b * (P * TYPES), P * TYPES), :]
                                     .rearrange("(p t) f -> p (t f)", t=TYPES)).then_inc(s_zl[k][q], 16)
                    sp.wait_ge(s_fin, 2 * i + k + 1)
                    sp.dma_start(tl[k], xres[bass.ds(b * P, P), :]).then_inc(s_zl[k][2], 16)

            def tail_out(i, last=False):
                for k in range(2):
                    b = 2 * i + k
                    n = LAST_ROWS if last and k else P
                    sp.wait_ge(s_fin, 2 * i + k + 3)
                    sp.dma_start(out[bass.ds(b * P, n), :], tl[2 + k][0:n, :]).then_inc(s_out[k], 16)

            tail_in(0)
            with sp.Fori(0, N_BLOCKS // 2 - 1) as i:
                tail_in(i + 1)
                tail_out(i)
            tail_out(N_BLOCKS // 2 - 1, last=True)
            for k in range(2):
                sp.wait_ge(s_out[k], 16 * (N_BLOCKS // 2))

        @block.gpsimd
        def _(pool):
            pool.iota(iota_i[:, :], pattern=[[1, P]], base=0, channel_multiplier=0).then_inc(s_iota, 1)
            pool.iota(part_i[:, :], pattern=[[0, 1]], base=0, channel_multiplier=1).then_inc(s_iota, 1)
            pool.memset(zero[:, :], 0.0).then_inc(s_zeroed, 1)
            pool.wait_ge(s_start, 1)
            at = bass.IndirectOffsetOnAxis(ap=st_u[0:EXTRA, 0:1], axis=0)
            for k, a in enumerate((dst, src, etype)):
                pool.indirect_dma_start(exn_i[0:EXTRA, k, :], None, a.rearrange("(c e) -> c e", e=P), at) \
                    .then_inc(s_exd, 16)
            pool.indirect_dma_start(exn[0:EXTRA, 2, :], None, ew.rearrange("(c e) -> c e", e=P), at) \
                .then_inc(s_exd, 16)

            for p in range(2):
                for k in range(2):
                    pool.wait_ge(s_st[k] if p == 0 else s_ns[0][k], 32 * (GROUPS // 2))
                with pool.Fori(0, ITER) as i:
                    for j in range(UNROLL):
                        if j % 4 == 0:
                            pool.wait_ge(s_ix[p], 2 * i + j // 4 + 1)
                            pool.sem_inc(tick, 1)
                        pool.indirect_dma_start(V[:, j, :], None, tabs[p],
                                                bass.IndirectOffsetOnAxis(ap=idx_r[:, j:j + 1], axis=0)) \
                            .then_inc(g_sem[p][j], 16)

            pool.wait_ge(s_zz, 16 * (2 * ZD + 2))
            with pool.Fori(0, ITER) as i:
                for m in range(PAIRS):
                    pool.wait_ge(s_i, PAIRS * i + m + 1)
                    pool.wait_ge(s_vc, PAIRS * i + m + 1)
                    if m >= 2:
                        pool.wait_ge(s_zs[m - 2], 32 * i + 32)
                    else:
                        pool.wait_ge(s_zs[m + 2], 32 * i)
                    pool.sem_inc(tick, 1)
                    for a in range(2):
                        pool.indirect_dma_start(Z[m % 2], bass.IndirectOffsetOnAxis(ap=idx_p[:, m, a:a + 1], axis=0),
                                                Vp[:, m, a, :], None, compute_op=ALU.add).then_inc(s_zs[m], 16)

            for m in range(PAIRS):
                pool.wait_ge(s_zs[m], 32 * ITER)

            def tail(i):
                for k in range(2):
                    if not isinstance(i, int):
                        pool.wait_ge(s_ht, 2 * i + k - 1)
                    pool.tensor_copy(tl[9 + k], Yf[:, bass.ds((2 * i + k) * HW, D)]).then_inc(s_hs, 1)

            tail(0)
            with pool.Fori(1, N_BLOCKS // 2) as i:
                tail(i)

        @block.tensor
        def _(pe):
            pe.wait_ge(s_const, 1)
            pe.wait_ge(s_natv, 1)
            n = 0
            for a in (nat_w[0], nat_y[0], nat_y[3], nat_y[4]):
                if a is nat_y[3]:
                    pe.wait_ge(load[3], 16)
                for j0 in range(0, NATC, 4):
                    if n >= 2:
                        pe.wait_ge(s_tpc, n - 1)
                    for j in range(j0, min(j0 + 4, NATC)):
                        t = pe.transpose(bank[n % 2][:, (j - j0) * NATP:(j - j0 + 1) * NATP],
                                         a[:, j * P:(j + 1) * P], ident[0:NATP, 0:NATP])
                    t.then_inc(s_tp, 1)
                    n += 1

            hist = bank[2][:, 0:N_BLOCKS]
            pe.wait_ge(s_zeroed, 1)
            z = zero[0:NATP, :].bitcast(BF16)
            pe.matmul(hist, z[:, 0:P], z[:, 0:N_BLOCKS], start=True, stop=False)
            with pe.Fori(0, NATW // UNROLL) as i:
                for j in range(UNROLL):
                    pe.wait_ge(s_oh, UNROLL * i + j + 1)
                    pe.matmul(hist, oh_lo[:, j, :], oh_hi[:, j, :], start=False, stop=False).then_inc(s_hm, 1)
            pe.matmul(hist, z[:, 0:P], z[:, 0:N_BLOCKS], start=False, stop=True).then_inc(s_hm, 1)
            pe.wait_ge(s_cnt, 1)
            pe.matmul(bank[3][0:N_BLOCKS, 0:1], cnt[:, :], ones[:, :], start=True, stop=True).then_inc(s_pfx, 1)
            pe.wait_ge(s_tot, 1)
            pe.matmul(bank[3][0:EXTRA, 1:2], later[0:N_BLOCKS, 1:N_BLOCKS], tot[0:N_BLOCKS, :],
                      start=True, stop=True).then_inc(s_pfx, 1)
            pe.wait_ge(s_exv, 1)
            for k in range(4):
                t = pe.transpose(bank[4][:, k * P:k * P + EXTRA], exn[0:EXTRA, k, :], ident[0:EXTRA, 0:EXTRA])
            t.then_inc(s_tp, 1)

            for p in range(2):
                pe.sem_inc(s_pm[p], UNROLL)
                with pe.Fori(0, ITER) as i:
                    for j in range(UNROLL):
                        pe.wait_ge(g_sem[p][j], 16 * i + 16)
                        pe.wait_ge(s_o[p], UNROLL * i + j + 1)
                        pe.matmul(bank[j][:, 0:D], O[:, j, :], V[:, j, :], start=True, stop=True) \
                            .then_inc(s_pm[p], 1)

            pe.wait_ge(s_np[1], 4 * (GROUPS // 2) + 2)
            pe.sem_inc(s_mm, PAIRS)

            def sums(i, m):
                pe.wait_ge(s_s, PAIRS * i + m + 1 + PAIRS)
                if m >= 2 or not isinstance(i, int):
                    pe.wait_ge(s_mc, PAIRS * i + m - 1)
                pe.matmul(bank[m % 2][:, 0:P], O[:, 2 * m, :], S[:, m, 0:P], start=True, stop=True)
                pe.matmul(bank[m % 2][:, P:3 * P], O[:, 2 * m + 1, :], S[:, m, P:3 * P],
                          start=True, stop=True).then_inc(s_mm, 1)

            def edge_rows(count, m, ba, bb, free):
                pe.wait_ge(s_mc, count)
                if free is not None:
                    pe.wait_ge(s_vc, free)
                ha, hb = Yf[:, bass.ds(ba * HW, HW)], Yf[:, bass.ds(bb * HW, HW)]
                pv = bank[2 + m % 2]
                pe.matmul(pv[:, 0:HW], M[:, m, 0:P], ha, start=True, stop=False)
                pe.matmul(pv[:, 0:HW], M[:, m, P:2 * P], hb, start=False, stop=True)
                pe.matmul(pv[:, HW:2 * HW], M[:, m, 2 * P:3 * P], hb, start=True, stop=True).then_inc(s_vm, 1)

            def layer1(i):
                first = isinstance(i, int)
                packed = [pe.value_load(pack_b[0:1, bass.ds(2 * i + k, 1)], min_val=0, max_val=(1 << 28) - 1)
                          for k in range(2)]
                for m in range(PAIRS):
                    sums(i, m)
                    if first and m == 0:
                        continue
                    r = packed[m // 2]
                    k = 2 * (m % 2)
                    ba, bb = ((r >> (7 * k)) % P if k else r % P), (r >> (7 * k + 7)) % P
                    n = PAIRS * i + m
                    edge_rows(n, (m - 1) % PAIRS, ba, bb, n - 2 if not first or m > 2 else None)

            layer1(0)
            with pe.Fori(1, ITER) as i:
                layer1(i)
            edge_rows(PAIRS * ITER, PAIRS - 1, 0, 0, PAIRS * ITER - 2)

            def tail(i):
                for k in range(2):
                    zs = zbuf[k][0].rearrange("p (t f) -> p t f", t=TYPES)
                    pe.wait_ge(s_zsum, 2 * i + k + 1)
                    for q in range(4):
                        n = 8 * i + 4 * k + q
                        if not isinstance(i, int) or k:
                            pe.wait_ge(s_ztc, n - 3)
                        for t in range(4):
                            tr = pe.transpose(bank[q][:, t * P:(t + 1) * P], zs[:, 4 * q + t, 0:D], ident[:, :])
                        tr.then_inc(s_zt, 1)
                    if not isinstance(i, int) or k:
                        pe.wait_ge(s_htc, 2 * i + k)
                    pe.wait_ge(s_hs, 2 * i + k + 1)
                    pe.transpose(bank[4][:, 0:P], tl[9 + k], ident[:, :]).then_inc(s_ht, 1)
                    pe.wait_ge(s_fin, 2 * i + k + 1)
                    for t in range(TYPES):
                        if t % 4 == 0:
                            pe.wait_ge(s_ztc, 8 * i + 4 * k + t // 4 + 1)
                        pe.matmul(bank[5 + k][:, 0:D], zt[:, t, :], wmat[:, t, :], start=t == 0, stop=t == TYPES - 1)
                    pe.wait_ge(s_htc, 2 * i + k + 1)
                    pe.matmul(bank[5 + k][:, D:2 * D], tl[4 + k], wself[:, :], start=True, stop=True) \
                        .then_inc(s_po, 1)

            tail(0)
            with pe.Fori(1, N_BLOCKS // 2) as i:
                tail(i)

        @block.scalar
        def _(act):
            n = 0
            for t in (src_t, rel_t, wgt_t, key_t):
                to = t[:, 0:CHUNKS].rearrange("p (q j) -> p j q", j=NATC)
                for j0 in range(0, NATC, 4):
                    w = min(4, NATC - j0)
                    act.wait_ge(s_tp, n + 1)
                    act.copy(to[:, j0:j0 + w, :], bank[n % 2][:, 0:w * NATP].rearrange("p (j q) -> p j q", j=w)) \
                        .then_inc(s_tpc, 1)
                    n += 1

            def root(phase, count, a):
                act.wait_ge(ask[phase], count)
                act.sem_inc(tick_a, 1)
                act.activation(a, a, ACT.Sqrt).then_inc(got[phase], 1)

            root(0, 1, dinv[:, :])
            act.wait_ge(s_tp, n + 1)
            for k, t in enumerate((src_t, rel_t, wgt_t, key_t)):
                act.copy(t[:, CHUNKS:STEPS], bank[4][:, k * P:k * P + EXTRA]).then_inc(s_tpc, 1)

            with act.Fori(0, GROUPS) as g:
                root(1, g + 1, stat[:, 1, :])

            act.wait_ge(s_tpc, 32)
            act.wait_ge(s_dummy, 4)
            for p in range(2):
                with act.Fori(0, ITER) as i:
                    for h in range(2):
                        act.wait_ge(s_pm[p], UNROLL * i + 4 * h + 4)
                        act.sem_inc(tick_a, 1)
                        act.copy(idx_r[:, 4 * h:4 * h + 4], src_t[:, bass.ds(UNROLL * i + 4 * h, 4)]) \
                            .then_inc(s_ix[p], 1)

            with act.Fori(0, GROUPS) as g:
                root(2, g + 1, stat[:, 1, :])

            def copy_rows(count, m):
                act.wait_ge(s_vm, count)
                act.copy(Vp[:, m, :, 0:HW], bank[2 + m % 2][:, 0:2 * HW].rearrange("p (a f) -> p a f", a=2)) \
                    .then_inc(s_vc, 1)

            def layer1(i):
                for m in range(PAIRS):
                    act.wait_ge(s_mm, PAIRS * i + m + 1 + PAIRS)
                    if not isinstance(i, int):
                        act.wait_ge(s_vm, PAIRS * i + m - 3)
                    act.copy(M[:, m, :], bank[m % 2][:, 0:3 * P]).then_inc(s_mc, 1)
                    if isinstance(i, int) and m == 0:
                        continue
                    if not isinstance(i, int):
                        q = (m - 1) % PAIRS
                        act.wait_ge(s_zs[q], 32 * i if m else 32 * i - 32)
                    copy_rows(PAIRS * i + m, (m - 1) % PAIRS)

            act.wait_ge(s_vpz, 1)
            layer1(0)
            with act.Fori(1, ITER) as i:
                layer1(i)
            act.wait_ge(s_zs[PAIRS - 1], 32 * ITER - 32)
            copy_rows(PAIRS * ITER, PAIRS - 1)

            def tail(i):
                for k in range(2):
                    for q in range(4):
                        act.wait_ge(s_zt, 8 * i + 4 * k + q + 1)
                        if not isinstance(i, int) or k:
                            act.wait_ge(s_po, 2 * i + k)
                        act.copy(zt[:, 4 * q:4 * q + 4, :],
                                 bank[q][:, :].rearrange("p (t n) -> p t n", t=4)).then_inc(s_ztc, 1)
                    act.wait_ge(s_ht, 2 * i + k + 1)
                    act.copy(tl[4 + k], bank[4][:, 0:P]).then_inc(s_htc, 1)
                    if not isinstance(i, int) or k:
                        root(3, 2 * i + k, stat[:, 6, 0:1])

            tail(0)
            with act.Fori(1, N_BLOCKS // 2) as i:
                tail(i)
            root(3, N_BLOCKS, stat[:, 6, 0:1])

        @block.vector
        def _(dve):
            link = Links(dve, s_dve)
            dve.wait_ge(s_iota, 2)
            link(dve.tensor_copy(iota_f[:, :], iota_i[:, :]))
            link(dve.tensor_copy(part_f[:, :], part_i[:, :]))
            link(dve.tensor_copy(iota_b[:, :], iota_f[:, :]))
            link(dve.tensor_scalar(later[:, :], iota_f[:, :], part_f[:, 0:1], None, ALU.is_gt))
            link(dve.memset(seen[:, 0:P], 1.0))
            link(dve.tensor_scalar(seen[:, P:2 * P], iota_f[:, :], part_f[:, 0:1], None, ALU.is_lt))
            link(dve.memset(ones[:, :], 1.0))
            link(dve.tensor_scalar(trash[:, 0:1], part_f[:, :], float(Z_ROWS), None, ALU.add))
            link(dve.tensor_scalar(trash[:, 1:2], part_f[:, :], float(Z_ROWS + P), None, ALU.add))
            link(dve.tensor_scalar(lo128[:, :], part_f[:, :], 128.0, 128.0, ALU.mult, ALU.add))
            link(dve.tensor_scalar(st_i[:, 2:3], part_f[:, :], 1.0, None, ALU.add))
            link(dve.tensor_scalar(ident[:, :], iota_f[:, :], part_f[:, 0:1], None, ALU.is_equal))
            dve.sem_inc(s_const, 1)

            dI, hiI = nat_w[0].bitcast(I32), nat_y[0].bitcast(I32)
            HI, LO, REL, SRC, KEY = nat_y[1], nat_y[2], nat_y[0], nat_w[0], nat_y[4]
            dve.wait_ge(load[0], 16)
            link(dve.tensor_single_scalar(hiI, dI, 7, ALU.arith_shift_right))
            link(dve.tensor_copy(HI, hiI))
            firsts = HI.rearrange("q (j e) -> q j e", e=P)[:, :, 0:1]
            link(dve.tensor_copy(blk_nat[:, :].rearrange("q (j o) -> q j o", o=1), firsts))
            link(dve.tensor_single_scalar(dI, dI, 127, ALU.bitwise_and))
            link(dve.tensor_copy(LO, dI))
            link(dve.tensor_tensor(REL.rearrange("q (j e) -> q j e", e=P), HI.rearrange("q (j e) -> q j e", e=P),
                                   firsts.to_broadcast([NATP, NATC, P]), ALU.subtract))
            link(dve.scalar_tensor_tensor(REL, REL, float(P), LO, ALU.mult, ALU.add))
            dve.wait_ge(load[1], 16)
            link(dve.tensor_copy(SRC, nat_y[4].bitcast(I32)))
            dve.wait_ge(load[2], 16)
            link(dve.tensor_copy(nat_w[1], nat_w[1].bitcast(I32)))
            link(dve.scalar_tensor_tensor(KEY, SRC, float(TYPES), nat_w[1], ALU.mult, ALU.add))
            dve.sem_inc(s_natv, 1)

            dve.wait_ge(load[4], 16)
            dve.wait_ge(load[5], 16)
            link.start()
            with dve.Fori(0, TYPES) as t:
                link.enter(t, BASES)
                o = wmat[:, bass.ds(t, 1), :].rearrange("p a f -> p (a f)")
                for b in range(BASES):
                    al = alph[:, bass.ds(t * BASES + b, 1)]
                    if b == 0:
                        link(dve.tensor_scalar(o, wb[:, b, :], al, None, ALU.mult))
                    else:
                        link(dve.scalar_tensor_tensor(o, wb[:, b, :], al, o, ALU.mult, ALU.add))
            link.leave(TYPES)
            for k in range(3):
                dve.wait_ge(load[7 + k], 16)
            link(dve.tensor_tensor(rows[:, 1, :], rows[:, 1, :], rows[:, 2, :], ALU.add))

            def onehots(i, first=False):
                for j in range(UNROLL):
                    if not first:
                        dve.wait_ge(s_hm, UNROLL * i + j - (UNROLL - 1))
                    dve.tensor_scalar(oh_lo[:, j, :], iota_b[0:NATP, :], LO[:, bass.ds(UNROLL * i + j, 1)], None,
                                      ALU.is_equal)
                    dve.tensor_scalar(oh_hi[:, j, :], iota_b[0:NATP, 0:N_BLOCKS], HI[:, bass.ds(UNROLL * i + j, 1)],
                                      None, ALU.is_equal).then_inc(s_oh, 1)

            onehots(0, True)
            with dve.Fori(1, NATW // UNROLL) as i:
                onehots(i)
            dve.wait_ge(s_hm, NATW + 1)
            link(dve.tensor_copy(cnt[:, :], bank[2][:, 0:N_BLOCKS]))
            dve.sem_inc(s_cnt, 1)
            link(dve.tensor_scalar(dtmp[:, :], cnt[:, :], 1.0, None, ALU.min))
            link(dve.tensor_scalar(dinv[:, :], cnt[:, :], 1.0, None, ALU.max))
            dve.sem_inc(ask[0], 1)
            dve.wait_ge(got[0], 1)
            link(dve.reciprocal(dinv[:, :], dinv[:, :]))
            link(dve.tensor_tensor(dinv[:, :], dinv[:, :], dtmp[:, :], ALU.mult))
            dve.wait_ge(s_pfx, 1)
            link(dve.tensor_copy(tot[0:N_BLOCKS, :], bank[3][0:N_BLOCKS, 0:1]))
            dve.sem_inc(s_tot, 1)
            dve.wait_ge(s_pfx, 2)
            link(dve.tensor_copy(st_i[0:EXTRA, 0:1], bank[3][0:EXTRA, 1:2]))
            link(dve.tensor_single_scalar(st_i[0:EXTRA, 1:2], st_i[0:EXTRA, 0:1], 127, ALU.bitwise_and))
            link(dve.tensor_single_scalar(st_i[0:EXTRA, 0:1], st_i[0:EXTRA, 0:1], 7, ALU.arith_shift_right))
            link(dve.tensor_scalar(st_u[0:EXTRA, :], st_i[0:EXTRA, 0:1], float(CHUNKS - 1), None, ALU.min))
            link(dve.tensor_scalar(st_ok[0:EXTRA, :], st_i[0:EXTRA, 1:2], 1.0, None, ALU.min))
            dve.sem_inc(s_start, 1)
            dve.wait_ge(s_exd, 64)
            link(dve.tensor_copy(exn[0:EXTRA, 1, :], exn_i[0:EXTRA, 0, :]))
            link(dve.tensor_scalar(exn[0:EXTRA, 1, :], exn[0:EXTRA, 1, :], lo128[0:EXTRA, 0:1], 1.0,
                                   ALU.subtract, ALU.add))
            link(dve.tensor_scalar(exn[0:EXTRA, 1, :], exn[0:EXTRA, 1, :], st_ok[0:EXTRA, 0:1], -1.0,
                                   ALU.mult, ALU.add))
            link(dve.tensor_copy(exn[0:EXTRA, 0, :], exn_i[0:EXTRA, 1, :]))
            link(dve.tensor_copy(exn[0:EXTRA, 3, :], exn_i[0:EXTRA, 2, :]))
            link(dve.scalar_tensor_tensor(exn[0:EXTRA, 3, :], exn[0:EXTRA, 0, :], float(TYPES), exn[0:EXTRA, 3, :],
                                          ALU.mult, ALU.add))
            dve.sem_inc(s_exv, 1)
            dve.memset(src_t[:, STEPS:STEPS_PAD], 0).then_inc(s_dummy, 1)
            dve.memset(rel_t[:, STEPS:STEPS_PAD + UNROLL], -1.0).then_inc(s_dummy, 1)
            dve.memset(wgt_t[:, STEPS:STEPS_PAD], 0.0).then_inc(s_dummy, 1)
            dve.memset(key_t[:, STEPS:STEPS_PAD], 0.0).then_inc(s_dummy, 1)
            dve.wait_ge(s_dummy, 4)
            dve.wait_ge(s_blkl, 16)
            for pk, o, n in ((pack_a, 2, STEPS_PAD // 4), (pack_b, 0, STEPS_PAD // 4 + 1)):
                v = blk_row[0:1, o:o + 4 * n].rearrange("p (w k) -> p w k", k=4)
                for k in range(1, 4):
                    link(dve.tensor_single_scalar(v[:, :, k], v[:, :, k], 7 * k, ALU.logical_shift_left))
                link(dve.tensor_tensor(pk[:, :], v[:, :, 0], v[:, :, 1], ALU.bitwise_or))
                link(dve.tensor_tensor(pk[:, :], pk[:, :], v[:, :, 2], ALU.bitwise_or))
                link(dve.tensor_tensor(pk[:, :], pk[:, :], v[:, :, 3], ALU.bitwise_or))
                for k in range(1, 4):
                    link(dve.tensor_single_scalar(v[:, :, k], v[:, :, k], 7 * k, ALU.logical_shift_right))
            dve.sem_inc(s_packed, 1)

            def dv(g):
                return dinv[:, bass.ds(g * GB, GB)]

            def wide(a):
                return a.unsqueeze(2).to_broadcast([P, GB, P])

            def layernorm(of, to, tmp, phase, count):
                s0, s1 = stat[:, 0, :], stat[:, 1, :]
                link(dve.tensor_reduce(s0, of, AX.X, ALU.add))
                link(dve.tensor_scalar(s0, s0, 1.0 / D, None, ALU.mult))
                link(dve.tensor_tensor(to, of, wide(s0), ALU.subtract))
                link(dve.tensor_tensor(tmp, to, to, ALU.mult))
                link(dve.tensor_reduce(s1, tmp, AX.X, ALU.add))
                link(dve.tensor_scalar(s1, s1, 1.0 / D, EPS, ALU.mult, ALU.add))
                dve.sem_inc(ask[phase], 1)
                dve.wait_ge(got[phase], count)
                link(dve.reciprocal(s1, s1))
                link(dve.tensor_tensor(tmp, to, wide(s1), ALU.mult))

            dve.wait_ge(s_tpc, 28)
            link(dve.memset(grp[0], 0.0))
            link(dve.memset(grp[1], 0.0))
            dve.sem_inc(s_ga, 2)

            def phase_a(i, last=False):
                for k in range(2):
                    dve.wait_ge(s_x[k], i * 16 + (32 if last and k else 16))
                    layernorm(grp[k], grp[6], grp[7], 1, 2 * i + k + 1)
                    link(dve.tensor_scalar(grp[6], grp[7], 0.0, None, ALU.max))
                    dve.wait_ge(s_st[k], 32 * i)
                    link(dve.scalar_tensor_tensor(grp[2 + k], grp[6], 1.0 / 3.0, grp[k], ALU.mult, ALU.add))
                    dve.sem_inc(s_ga, 1)
                    link(dve.tensor_tensor(grp[4 + k], grp[6], wide(dv(2 * i + k)), ALU.mult))
                    dve.sem_inc(s_ga, 1)

            link.start()
            with dve.Fori(0, GROUPS // 2 - 1) as i:
                link.enter(i, 22)
                phase_a(i)
            link.leave(GROUPS // 2 - 1)
            phase_a(GROUPS // 2 - 1, last=True)

            link(dve.memset(Yf, 0.0))
            for p in range(2):
                def onehot(i, j):
                    dve.wait_ge(s_pm[p], UNROLL * i + j + 1)
                    dve.tensor_scalar(O[:, j, :], iota_f[:, :], rel_t[:, bass.ds(UNROLL * i + j, 1)], None,
                                      ALU.is_equal).then_inc(s_o[p], 1)

                for j in range(UNROLL):
                    onehot(0, j)
                with dve.Fori(0, ITER) as i:
                    packed = [dve.value_load(pack_a[0:1, bass.ds(2 * i + k, 1)], min_val=0, max_val=(1 << 28) - 1)
                              for k in range(2)]
                    for j in range(UNROLL):
                        r, k = packed[j // 4], j % 4
                        b = (r >> (7 * k)) % P if k else r % P
                        y = Yf[:, bass.ds(b * HW, D)]
                        dve.wait_ge(s_pm[p], UNROLL * i + j + 1 + UNROLL)
                        dve.wait_ge(s_y[p], UNROLL * i + j)
                        dve.tensor_tensor(y, y, bank[j][:, 0:D], ALU.add).then_inc(s_y[p], 1)
                        onehot(i + 1, j)
                dve.wait_ge(s_y[p], UNROLL * ITER)
                dve.wait_ge(s_o[p], UNROLL * ITER + UNROLL)

                dve.sem_inc(s_np[p], 2)
                link.start()
                with dve.Fori(0, GROUPS // 2) as i:
                    link.enter(i, 8 if p == 0 else 24)
                    for k in range(2):
                        g = 2 * i + k
                        yg = Yf[:, bass.ds(g * (GB * HW), GB * HW)].rearrange("p (b f) -> p b f", f=HW)
                        yd = yg[:, :, 0:D]
                        link(dve.tensor_tensor(grp[6], yd, wide(dv(g)), ALU.mult))
                        dve.wait_ge(s_nx[p][k], 16 * i + 16)
                        dve.wait_ge(s_ns[p][k], (32 if p == 0 else 16) * i)
                        link(dve.scalar_tensor_tensor(grp[2 + k], grp[6], 1.0 / 3.0, grp[k], ALU.mult, ALU.add))
                        dve.sem_inc(s_np[p], 1)
                        if p == 0:
                            link(dve.tensor_tensor(grp[4 + k], grp[6], wide(dv(g)), ALU.mult))
                            link(dve.tensor_scalar(yd, zero[:, 0:GW].rearrange("p (b f) -> p b f", f=D), 0.0, None, ALU.add))
                        else:
                            layernorm(grp[2 + k], grp[6], grp[7], 2, 2 * i + k + 1)
                            link(dve.tensor_scalar(yd, grp[7], 0.0, None, ALU.max))
                            link(dve.tensor_scalar(yg[:, :, D:HW], zero[:, 0:GB].unsqueeze(2), 1.0, None, ALU.add))
                        dve.sem_inc(s_np[p], 1)
                link.leave(GROUPS // 2)

            for k in range(2):
                dve.wait_ge(s_ns[1][k], 16 * (GROUPS // 2))
            link(dve.memset(Vp[:, :, :, :], 0.0))
            dve.sem_inc(s_vpz, 1)
            dve.sem_inc(s_s, PAIRS)
            link.start()
            with dve.Fori(0, ITER) as i:
                link.enter(i, 5 * PAIRS)
                for m in range(PAIRS):
                    s = UNROLL * i + 2 * m
                    col = lambda t, k: t[:, bass.ds(s + k, 1)]
                    dve.wait_ge(s_mm, PAIRS * i + m + 1)
                    for a in range(2):
                        dve.tensor_scalar(O[:, 2 * m + a, :], iota_f[:, :], col(rel_t, a), col(wgt_t, a),
                                          ALU.is_equal, ALU.mult)
                    dve.wait_ge(s_kr[m], 16 * i + 16)
                    dve.tensor_scalar(S[:, m, 0:P], krow[:, m, 0:P], col(key_t, 0), None, ALU.is_equal)
                    dve.tensor_scalar(S[:, m, P:3 * P], krow[:, m, :], col(key_t, 1), None, ALU.is_equal) \
                        .then_inc(s_s, 1)
                    dve.wait_ge(s_s, PAIRS * i + m + 1 + PAIRS)
                    dve.tensor_tensor_reduce(out=junk[:, 0:P], in0=S[:, m, 0:P], in1=seen[:, P:2 * P], scale=1.0,
                                             scalar=0.0, op0=ALU.mult, op1=ALU.add,
                                             accum_out=dup[:, m, 0:1]).then_inc(s_dve, 1)
                    link.at += 1
                    link(dve.tensor_tensor(dif[:, m, :], trash[:, :], key_t[:, bass.ds(s, 2)], ALU.subtract))
                    link(dve.tensor_tensor_reduce(out=junk[:, :], in0=S[:, m, P:3 * P], in1=seen[:, :], scale=1.0,
                                                  scalar=0.0, op0=ALU.mult, op1=ALU.add,
                                                  accum_out=dup[:, m, 1:2]))
                    link(dve.scalar_tensor_tensor(dif[:, m, :], dup[:, m, :], 1.0, dif[:, m, :], ALU.min, ALU.mult))
                    dve.wait_ge(s_zs[m], 32 * i)
                    link(dve.tensor_tensor(idx_p[:, m, :], dif[:, m, :], key_t[:, bass.ds(s, 2)], ALU.add))
                    dve.sem_inc(s_i, 1)
            link.leave(ITER)

            dve.sem_inc(s_fin, 2)

            def z_sum(i, k):
                for q in range(2):
                    dve.wait_ge(s_zl[k][q], 16 * i + 16)
                link(dve.tensor_tensor(zbuf[k][0], zbuf[k][0], zbuf[k][1], ALU.add))
                zs = zbuf[k][0].rearrange("p (t f) -> p t f", t=TYPES)
                link(dve.tensor_reduce(stat[:, 3 + k, 0:1], zs[:, :, D], AX.X, ALU.add))
                dve.sem_inc(s_zsum, 1)

            def finish(i, k):
                t1, t2, t3 = tl[6], tl[7], tl[8]
                deg, mean, var = stat[:, 3 + k, 0:1], stat[:, 5, 0:1], stat[:, 6, 0:1]
                link(dve.tensor_scalar(deg, deg, 1e-12, None, ALU.max))
                link(dve.reciprocal(deg, deg))
                dve.wait_ge(s_po, 2 * i + k + 1)
                link(dve.tensor_scalar(t1, bank[5 + k][:, 0:D], deg, None, ALU.mult))
                link(dve.tensor_reduce(mean, t1, AX.X, ALU.add))
                link(dve.tensor_scalar(mean, mean, 1.0 / D, None, ALU.mult))
                link(dve.tensor_scalar(t2, t1, mean, None, ALU.subtract))
                link(dve.tensor_tensor_reduce(out=t3, in0=t2, in1=t2, scale=1.0, scalar=0.0, op0=ALU.mult,
                                              op1=ALU.add, accum_out=var))
                link(dve.tensor_scalar(var, var, 1.0 / D, EPS, ALU.mult, ALU.add))
                dve.sem_inc(ask[3], 1)
                dve.wait_ge(got[3], 2 * i + k + 1)
                link(dve.reciprocal(var, var))
                link(dve.scalar_tensor_tensor(t1, t2, var, rows[:, 0, :], ALU.mult, ALU.mult))
                link(dve.tensor_tensor(t2, t1, rows[:, 1, :], ALU.add))
                link(dve.tensor_tensor(t1, t2, bank[5 + k][:, D:2 * D], ALU.add))
                dve.wait_ge(s_zl[k][2], 16 * i + 16)
                dve.wait_ge(s_out[k], 16 * i)
                link(dve.tensor_tensor(tl[2 + k], t1, tl[k], ALU.add))
                dve.sem_inc(s_fin, 1)

            z_sum(0, 0)
            link.start()
            with dve.Fori(0, N_BLOCKS // 2 - 1) as i:
                link.enter(i, 30)
                z_sum(i, 1)
                finish(i, 0)
                z_sum(i + 1, 0)
                finish(i, 1)
            link.leave(N_BLOCKS // 2 - 1)
            z_sum(N_BLOCKS // 2 - 1, 1)
            for k in range(2):
                finish(N_BLOCKS // 2 - 1, k)


_INS = ["x", "src", "dst", "edge_type_16", "edge_weight", "L1_gnn_weight", "L1_gnn_alpha", "L1_gnn_bias",
        "L1_gnn_w_self", "L1_gnn_ln_gamma", "L1_gnn_ln_beta"]


def kernel(**inputs):
    import concourse.bacc as bacc
    from concourse.bass_utils import run_bass_kernel_spmd

    nc = bacc.Bacc("TRN2", target_bir_lowering=False, num_devices=1)
    arrays, args = {}, []
    for name in _INS:
        a = np.ascontiguousarray(inputs[name])
        arrays[f"in_{name}"] = a
        args.append(nc.dram_tensor(f"in_{name}", a.shape, mybir.dt.from_np(a.dtype), kind="ExternalInput").ap())
    x = args[0]
    o = nc.dram_tensor("out_0", x.shape, F32, kind="ExternalOutput").ap()
    build(nc, *args, o)
    r = run_bass_kernel_spmd(nc, [arrays], core_ids=[0])
    return r.results[0]["out_0"]
```
